# Optimizing a Trainium2 kernel written in Bass

```python
import numpy as np
import jax
import jax.numpy as jnp

def _softmax(x, axis=-1):
    return jax.nn.softmax(x, axis=axis)

def _gelu(x):
    return jax.nn.gelu(x, approximate=True)

def _silu(x):
    return jax.nn.silu(x)

def _sigmoid(x):
    return jax.nn.sigmoid(x)

def _layernorm(x, axis=-1, eps=1e-05):
    m = jnp.mean(x, axis=axis, keepdims=True)
    v = jnp.var(x, axis=axis, keepdims=True)
    return (x - m) / jnp.sqrt(v + eps)

def _scatter_add(tgt, idx, src, axis=0):
    return tgt.at[idx].add(src)

def _segment_sum(src, seg, n):
    return jax.ops.segment_sum(src, seg, n)
kernel_name = 'mk_seq_postln_d2_jaxref_r8_3cc907'

def setup_inputs(seed: int=0):
    np.random.seed(seed)
    _w = jnp.asarray

    def _L0_attn_setup():
        import jax, jax.numpy as jnp
        import numpy as np
        B, S, E, H = (2, 256, 128, 16)
        HD = E // H
        LAMBDA_INIT = 0.8
        EPS = 1e-06
        key = jax.random.key(seed)
        ks = jax.random.split(key, 8)
        return {'x': jax.random.normal(ks[0], (B, S, E), dtype=jnp.float32), 'w_qkv': jax.random.normal(ks[1], (E, 3 * E), dtype=jnp.float32) * E ** (-0.5), 'wo': jax.random.normal(ks[2], (E, E), dtype=jnp.float32) * E ** (-0.5), 'lambda_q1': jax.random.normal(ks[3], (HD,), dtype=jnp.float32) * 0.1, 'lambda_q2': jax.random.normal(ks[4], (HD,), dtype=jnp.float32) * 0.1, 'lambda_k1': jax.random.normal(ks[5], (HD,), dtype=jnp.float32) * 0.1, 'lambda_k2': jax.random.normal(ks[6], (HD,), dtype=jnp.float32) * 0.1, 'norm_w': jnp.ones((H, HD), dtype=jnp.float32)}
    _L0_attn_in = _L0_attn_setup()

    def _L0_ffn_setup():
        import jax, jax.numpy as jnp
        import numpy as np
        BLOCK = 16
        _GRID = jnp.array([0.0, 0.5, 1.0, 1.5, 2.0, 3.0, 4.0, 6.0], dtype=jnp.float32)
        _MID = jnp.array([0.25, 0.75, 1.25, 1.75, 2.5, 3.5, 5.0], dtype=jnp.float32)

        def fp4_quant_dequant(x):
            shape = x.shape
            xb = x.reshape(shape[:-1] + (shape[-1] // BLOCK, BLOCK))
            scale = jnp.max(jnp.abs(xb), axis=-1, keepdims=True) / 6.0
            scale = jnp.maximum(scale, jnp.float32(1e-12))
            xn = xb / scale
            idx = jnp.searchsorted(_MID, jnp.abs(xn))
            q = _GRID[idx] * jnp.sign(xn) * scale
            return q.reshape(shape)

        def fp4_linear(x, w):
            xq = fp4_quant_dequant(x)
            wq = fp4_quant_dequant(w)
            return jnp.einsum('bsk,nk->bsn', xq, wq)
        key = jax.random.key(seed)
        k1, k2, k3, k4 = jax.random.split(key, 4)
        H, I = (128, 352)
        x = jax.random.normal(k1, (4, 512, H), dtype=jnp.float32)
        w_gate = jax.random.normal(k2, (I, H), dtype=jnp.float32) * 0.02
        w_up = jax.random.normal(k3, (I, H), dtype=jnp.float32) * 0.02
        w_down = jax.random.normal(k4, (H, I), dtype=jnp.float32) * 0.02
        return {'x': x, 'w_gate': w_gate, 'w_up': w_up, 'w_down': w_down}
    _L0_ffn_in = _L0_ffn_setup()

    def _L1_attn_setup():
        import jax, jax.numpy as jnp
        import numpy as np
        EMB = 128
        NQ = 16
        NKV = 4
        D = 64
        B, S = (1, 256)
        ROPE_BASE = 10000.0

        def _rotary(t):
            d = t.shape[-1]
            inv_freq = 1.0 / ROPE_BASE ** (jnp.arange(0, d, 2, dtype=jnp.float32) / d)
            pos = jnp.arange(t.shape[1], dtype=jnp.float32)
            ang = pos[:, None] * inv_freq[None, :]
            cos = jnp.concatenate([jnp.cos(ang), jnp.cos(ang)], axis=-1)[None, :, None, :]
            sin = jnp.concatenate([jnp.sin(ang), jnp.sin(ang)], axis=-1)[None, :, None, :]
            x1, x2 = (t[..., :d // 2], t[..., d // 2:])
            t_rot = jnp.concatenate([-x2, x1], axis=-1)
            return t * cos + t_rot * sin
        key = jax.random.key(seed)
        ks = jax.random.split(key, 5)
        std = 0.02
        return {'x': jax.random.normal(ks[0], (B, S, EMB), jnp.float32), 'Wq': jax.random.normal(ks[1], (EMB, NQ * D), jnp.float32) * std, 'bq': jnp.zeros((NQ * D,), jnp.float32), 'Wk': jax.random.normal(ks[2], (EMB, NKV * D), jnp.float32) * std, 'bk': jnp.zeros((NKV * D,), jnp.float32), 'Wv': jax.random.normal(ks[3], (EMB, NKV * D), jnp.float32) * std, 'bv': jnp.zeros((NKV * D,), jnp.float32), 'Wo': jax.random.normal(ks[4], (NQ * D, EMB), jnp.float32) * std, 'bo': jnp.zeros((EMB,), jnp.float32)}
    _L1_attn_in = _L1_attn_setup()

    def _L1_ffn_setup():
        import jax, jax.numpy as jnp
        import numpy as np
        B, S, D, F, E = (4, 256, 128, 512, 8)
        LN_EPS = 1e-05
        key = jax.random.key(seed)
        ks = jax.random.split(key, 6)
        sc = 0.02
        return {'x': jax.random.normal(ks[0], (B, S, D), dtype=jnp.float32), 'Wr': jax.random.normal(ks[1], (D, E), dtype=jnp.float32) * sc, 'br': jnp.zeros((E,), jnp.float32), 'ln_g': jnp.ones((D,), jnp.float32), 'ln_b': jnp.zeros((D,), jnp.float32), 'W1': jax.random.normal(ks[2], (E, D, F), dtype=jnp.float32) * sc, 'b1': jnp.zeros((E, F), jnp.float32), 'W2': jax.random.normal(ks[3], (E, F, D), dtype=jnp.float32) * sc, 'b2': jnp.zeros((E, D), jnp.float32)}
    _L1_ffn_in = _L1_ffn_setup()
    _d = {'L0_attn_x': _L0_attn_in['x'], 'L0_attn_w_qkv': _L0_attn_in['w_qkv'], 'L0_attn_wo': _L0_attn_in['wo'], 'L0_attn_lambda_q1': _L0_attn_in['lambda_q1'], 'L0_attn_lambda_q2': _L0_attn_in['lambda_q2'], 'L0_attn_lambda_k1': _L0_attn_in['lambda_k1'], 'L0_attn_lambda_k2': _L0_attn_in['lambda_k2'], 'L0_attn_norm_w': _L0_attn_in['norm_w'], 'L0_ffn_w_gate': _L0_ffn_in['w_gate'], 'L0_ffn_w_up': _L0_ffn_in['w_up'], 'L0_ffn_w_down': _L0_ffn_in['w_down'], 'L1_attn_Wq': _L1_attn_in['Wq'], 'L1_attn_bq': _L1_attn_in['bq'], 'L1_attn_Wk': _L1_attn_in['Wk'], 'L1_attn_bk': _L1_attn_in['bk'], 'L1_attn_Wv': _L1_attn_in['Wv'], 'L1_attn_bv': _L1_attn_in['bv'], 'L1_attn_Wo': _L1_attn_in['Wo'], 'L1_attn_bo': _L1_attn_in['bo'], 'L1_ffn_Wr': _L1_ffn_in['Wr'], 'L1_ffn_br': _L1_ffn_in['br'], 'L1_ffn_ln_g': _L1_ffn_in['ln_g'], 'L1_ffn_ln_b': _L1_ffn_in['ln_b'], 'L1_ffn_W1': _L1_ffn_in['W1'], 'L1_ffn_b1': _L1_ffn_in['b1'], 'L1_ffn_W2': _L1_ffn_in['W2'], 'L1_ffn_b2': _L1_ffn_in['b2']}
    _x0 = _d['L0_attn_x']
    _d['L0_attn_x'] = jax.random.normal(jax.random.fold_in(jax.random.key(seed), 1), (4, 512, 128), dtype=_x0.dtype)
    del _x0
    return _d

def reference(L0_attn_x, L0_attn_w_qkv, L0_attn_wo, L0_attn_lambda_q1, L0_attn_lambda_q2, L0_attn_lambda_k1, L0_attn_lambda_k2, L0_attn_norm_w, L0_ffn_w_gate, L0_ffn_w_up, L0_ffn_w_down, L1_attn_Wq, L1_attn_bq, L1_attn_Wk, L1_attn_bk, L1_attn_Wv, L1_attn_bv, L1_attn_Wo, L1_attn_bo, L1_ffn_Wr, L1_ffn_br, L1_ffn_ln_g, L1_ffn_ln_b, L1_ffn_W1, L1_ffn_b1, L1_ffn_W2, L1_ffn_b2):

    def _L0_attn_ref(x, w_qkv, wo, lambda_q1, lambda_q2, lambda_k1, lambda_k2, norm_w):
        import jax, jax.numpy as jnp
        import numpy as np
        B, S, E, H = (2, 256, 128, 16)
        HD = E // H
        LAMBDA_INIT = 0.8
        EPS = 1e-06
        b, s, e = x.shape
        qkv = x @ w_qkv
        q, k, v = jnp.split(qkv, 3, axis=-1)

        def to_heads(t):
            return t.reshape(b, s, H, HD).transpose(0, 2, 1, 3)
        q, k, v = (to_heads(q), to_heads(k), to_heads(v))
        q1, q2 = jnp.split(q, 2, axis=-1)
        k1, k2 = jnp.split(k, 2, axis=-1)
        scale = 1.0 / jnp.sqrt(jnp.asarray(HD, dtype=x.dtype))
        a1 = jax.nn.softmax(jnp.einsum('bhsd,bhtd->bhst', q1, k1) * scale, axis=-1)
        a2 = jax.nn.softmax(jnp.einsum('bhsd,bhtd->bhst', q2, k2) * scale, axis=-1)
        lam = jnp.exp(jnp.dot(lambda_q1, lambda_k1)) - jnp.exp(jnp.dot(lambda_q2, lambda_k2)) + LAMBDA_INIT
        a = a1 - lam * a2
        out = jnp.einsum('bhst,bhtd->bhsd', a, v)
        rms = jnp.sqrt(jnp.mean(out * out, axis=-1, keepdims=True) + EPS)
        out_n = out / rms * norm_w[None, :, None, :] * (1.0 - LAMBDA_INIT)
        out_cat = out_n.reshape(b, H * s, HD)
        out_final = out_cat.transpose(0, 2, 1).reshape(b, s, e)
        return out_final @ wo

    def _L0_ffn_ref(x, w_gate, w_up, w_down):
        import jax, jax.numpy as jnp
        import numpy as np
        BLOCK = 16
        _GRID = jnp.array([0.0, 0.5, 1.0, 1.5, 2.0, 3.0, 4.0, 6.0], dtype=jnp.float32)
        _MID = jnp.array([0.25, 0.75, 1.25, 1.75, 2.5, 3.5, 5.0], dtype=jnp.float32)

        def fp4_quant_dequant(x):
            shape = x.shape
            xb = x.reshape(shape[:-1] + (shape[-1] // BLOCK, BLOCK))
            scale = jnp.max(jnp.abs(xb), axis=-1, keepdims=True) / 6.0
            scale = jnp.maximum(scale, jnp.float32(1e-12))
            xn = xb / scale
            idx = jnp.searchsorted(_MID, jnp.abs(xn))
            q = _GRID[idx] * jnp.sign(xn) * scale
            return q.reshape(shape)

        def fp4_linear(x, w):
            xq = fp4_quant_dequant(x)
            wq = fp4_quant_dequant(w)
            return jnp.einsum('bsk,nk->bsn', xq, wq)
        gate = fp4_linear(x, w_gate)
        y = fp4_linear(x, w_up)
        h = jax.nn.silu(gate) * y
        return fp4_linear(h, w_down)

    def _L1_attn_ref(x, Wq, bq, Wk, bk, Wv, bv, Wo, bo):
        import jax, jax.numpy as jnp
        import numpy as np
        EMB = 128
        NQ = 16
        NKV = 4
        D = 64
        B, S = (1, 256)
        ROPE_BASE = 10000.0

        def _rotary(t):
            d = t.shape[-1]
            inv_freq = 1.0 / ROPE_BASE ** (jnp.arange(0, d, 2, dtype=jnp.float32) / d)
            pos = jnp.arange(t.shape[1], dtype=jnp.float32)
            ang = pos[:, None] * inv_freq[None, :]
            cos = jnp.concatenate([jnp.cos(ang), jnp.cos(ang)], axis=-1)[None, :, None, :]
            sin = jnp.concatenate([jnp.sin(ang), jnp.sin(ang)], axis=-1)[None, :, None, :]
            x1, x2 = (t[..., :d // 2], t[..., d // 2:])
            t_rot = jnp.concatenate([-x2, x1], axis=-1)
            return t * cos + t_rot * sin
        b, s, _ = x.shape
        g = NQ // NKV
        q = (x @ Wq + bq).reshape(b, s, NQ, D)
        k = (x @ Wk + bk).reshape(b, s, NKV, D)
        v = (x @ Wv + bv).reshape(b, s, NKV, D)
        q = _rotary(q)
        k = _rotary(k)
        qg = q.reshape(b, s, NKV, g, D)
        scale = 1.0 / jnp.sqrt(jnp.float32(D))
        logits = jnp.einsum('bqhgd,bkhd->bhgqk', qg, k) * scale
        causal = jnp.tril(jnp.ones((s, s), bool))
        logits = jnp.where(causal, logits, jnp.float32(-1e+30))
        w = jax.nn.softmax(logits, axis=-1)
        out = jnp.einsum('bhgqk,bkhd->bqhgd', w, v).reshape(b, s, NQ * D)
        return out @ Wo + bo

    def _L1_ffn_ref(x, Wr, br, ln_g, ln_b, W1, b1, W2, b2):
        import jax, jax.numpy as jnp
        import numpy as np
        B, S, D, F, E = (4, 256, 128, 512, 8)
        LN_EPS = 1e-05
        tokens_shape = x.shape[:-1]
        xt = x.reshape(-1, x.shape[-1])
        router_logits = xt @ Wr + br
        router_probs = jax.nn.softmax(router_logits, axis=-1)
        gates = jnp.max(router_probs, axis=-1, keepdims=True)
        idx = jnp.argmax(router_probs, axis=-1)
        onehot = jax.nn.one_hot(idx, E, dtype=xt.dtype)
        mu = jnp.mean(xt, axis=-1, keepdims=True)
        var = jnp.mean(jnp.square(xt - mu), axis=-1, keepdims=True)
        xn = (xt - mu) * jax.lax.rsqrt(var + LN_EPS) * ln_g + ln_b
        h = jnp.einsum('te,td,edf->tf', onehot, xn, W1) + b1[idx]
        h = jax.nn.relu(h)
        y = jnp.einsum('te,tf,efd->td', onehot, h, W2) + b2[idx]
        y = y * gates
        return y.reshape(tokens_shape + (y.shape[-1],))
    x = L0_attn_x
    x = _layernorm(x + _L0_attn_ref(x, L0_attn_w_qkv, L0_attn_wo, L0_attn_lambda_q1, L0_attn_lambda_q2, L0_attn_lambda_k1, L0_attn_lambda_k2, L0_attn_norm_w), axis=-1)
    x = _layernorm(x + _L0_ffn_ref(x, L0_ffn_w_gate, L0_ffn_w_up, L0_ffn_w_down), axis=-1)
    x = _layernorm(x + _L1_attn_ref(x, L1_attn_Wq, L1_attn_bq, L1_attn_Wk, L1_attn_bk, L1_attn_Wv, L1_attn_bv, L1_attn_Wo, L1_attn_bo), axis=-1)
    x = _layernorm(x + _L1_ffn_ref(x, L1_ffn_Wr, L1_ffn_br, L1_ffn_ln_g, L1_ffn_ln_b, L1_ffn_W1, L1_ffn_b1, L1_ffn_W2, L1_ffn_b2), axis=-1)
    return x

_drawn_inputs = setup_inputs


def setup_inputs(seed=0):
    import zlib

    import numpy as np

    out = dict(_drawn_inputs(seed))
    spreads = {'L0_attn_norm_w': (1.0, 0.2),
     'L1_attn_bq': (0.0, 0.8),
     'L1_attn_bk': (0.0, 0.8),
     'L1_attn_bv': (0.0, 0.1),
     'L1_attn_bo': (0.0, 0.1),
     'L1_ffn_br': (0.0, 0.507),
     'L1_ffn_ln_g': (1.0, 0.6),
     'L1_ffn_ln_b': (0.0, 0.8),
     'L1_ffn_b1': (0.0, 0.8),
     'L1_ffn_b2': (0.0, 0.451)}
    factors = {'L0_attn_lambda_q1': 8.0,
     'L0_attn_lambda_q2': 8.0,
     'L0_attn_lambda_k1': 8.0,
     'L0_attn_lambda_k2': 6.535,
     'L0_ffn_w_gate': 5.443,
     'L0_ffn_w_up': 5.195,
     'L0_ffn_w_down': 5.171,
     'L1_attn_Wq': 8.0,
     'L1_attn_Wk': 8.0,
     'L1_attn_Wv': 3.533,
     'L1_ffn_W1': 5.196,
     'L1_ffn_W2': 4.043}
    for name, (base, spread) in spreads.items():
        noise = np.random.default_rng([zlib.crc32(name.encode()), seed]).standard_normal(out[name].shape)
        drawn = base * np.exp(spread * noise) if base else spread * noise
        out[name] = jnp.asarray(drawn.astype(out[name].dtype))
    for name, factor in factors.items():
        out[name] = (out[name] * factor).astype(out[name].dtype)
    return out
```

```python
from contextlib import ExitStack

import concourse.bass as bass
from concourse import mybir

ALU = mybir.AluOpType
ACT = mybir.ActivationFunctionType
AX = mybir.AxisListType.X
F32 = mybir.dt.float32
BF16 = mybir.dt.bfloat16
U32 = mybir.dt.uint32

P = 128
BATCH, T, E = 4, 512, 128
NT = T // P
H0, HD0 = 16, 8
NG = 8
HF = 4
NTERM = 6
Q_PART = (0, 0, 1, 1, 0, 2)
K_PART = (0, 1, 0, 1, 2, 0)
M_ROW = NTERM * 16
LAMBDA_INIT = 0.8
RMS_EPS = 1e-6
FF0 = 352
FCH = (128, 128, 96)
QB = 16
NQ, NKV, D1 = 16, 4, 64
WID = (512, 384, 256, 128)
POFF = (0, 512, 1024, 896)
PW = 1280
NE, FF1 = 8, 512
LN_EPS = 1e-5
NEG = -1e30
SIGN = 0x80000000


def build(nc, x, w_qkv, wo, lq1, lq2, lk1, lk2, norm_w, w_gate, w_up, w_down,
          Wq, bq, Wk, bk, Wv, bv, Wo, bo, Wr, br, ln_g, ln_b, W1, b1, W2, b2, const, rope, out):
    x_rows = x.rearrange("b (t p) e -> b p t e", p=P)
    out_rows = out.rearrange("b (t p) e -> b p t e", p=P)
    parts_dram = nc.dram_tensor("qk_parts", (2, 3, P, T), BF16, kind="Internal").ap()

    with ExitStack() as ctx:
        def sb(name, shape, dt=F32):
            return ctx.enter_context(nc.sbuf_tensor(name, shape, dt))

        row_signals = []

        def sem(name):
            return ctx.enter_context(nc.semaphore(name))

        def sig(name):
            row_signals.append(sem(name))
            return row_signals[-1]

        cst = sb("cst", [P, 3 * P + HF + 1 + NE])
        ident, jmask = cst[:, 0:P], cst[:, 3 * P:3 * P + HF]
        rot_sign, rank = cst[:, 3 * P + HF:3 * P + HF + 1], cst[:, 3 * P + HF + 1:]
        bmask = sb("bmask", [P, 3, P], BF16)
        identb, mask_qk, mask_kq = bmask[:, 0], bmask[:, 1], bmask[:, 2]
        rope_sb = sb("rope_sb", [P, 2, T])
        ones = sb("ones", [P, D1])
        ones3 = sb("ones3", [3, P], BF16)
        eps = sb("eps", [P, 2])
        wqkv_sb = sb("wqkv_sb", [P, 3 * E])
        wo0_sb = sb("wo0_sb", [P, E])
        lam_in = sb("lam_in", [P, 4, HD0])
        lam_w = sb("lam_w", [P, 2, HD0])
        lam_s = sb("lam_s", [P, 4])
        lam = sb("lam", [P, 1])
        nw_sb = sb("nw_sb", [P, P])
        wgT = sb("wgT", [P, 2, FF0])
        wdT = sb("wdT", [P, 3, E])
        wq_sb = sb("wq_sb", [P, 2, NQ * D1])
        wk_in = sb("wk_in", [P, NKV * D1])
        wk_sb = sb("wk_sb", [P, 2, NKV, 2, D1])
        wv_sb = sb("wv_sb", [P, NKV * D1])
        wo1_sb = sb("wo1_sb", [P, 8, E])
        bqk = sb("bqk", [P, 2, 12])
        bv_sb = sb("bv_sb", [P, NKV * D1])
        bo_sb = sb("bo_sb", [P, E])
        wr_sb = sb("wr_sb", [P, NE])
        br_sb = sb("br_sb", [P, NE])
        lng = sb("lng", [P, 2])
        w1_sb = sb("w1_sb", [P, NE, FF1])
        w2_sb = sb("w2_sb", [P, NE, FF1 // P, E])
        b1_sb = sb("b1_sb", [P, NE, FF1 // P])
        b2_sb = sb("b2_sb", [NE, E])
        X = sb("X", [P, NT, E])
        Z = sb("Z", [P, NT, E])
        ZS = sb("ZS", [P, NT, E])
        xT = sb("xT", [P, T])
        st = sb("st", [P, 4, NT])
        KPAD = sb("KPAD", [P, NG * HF * T], BF16)
        PROB = sb("PROB", [P, 2 * 4 * PW])
        SH = sb("SH", [P, 6144])
        kpad = KPAD[:, :].rearrange("p (g j n) -> p g j n", g=NG, j=HF)
        prob0 = PROB[:, 0:2 * HF * 2 * T].rearrange("p (s j k n) -> p s j k n", s=2, j=HF, k=2)
        prob1 = PROB[:, :].rearrange("p (s h n) -> p s h n", s=2, h=4)
        qst = SH[:, 0:2048].bitcast(BF16).rearrange("p (g n) -> p g n", g=NG)
        kst = SH[:, 2048:4096].bitcast(BF16).rearrange("p (g n) -> p g n", g=NG)
        split = SH[:, 4096:5632].bitcast(BF16).rearrange("p (c s n) -> p c s n", c=2, s=3)
        osb = SH[:, 5632:6144]
        rem = PROB[:, 0:2 * T].rearrange("p (c n) -> p c n", c=2)
        v0 = sb("v0", [P, NT, H0, 32])
        mx = sb("mx", [P, 2, 16])
        mrem = sb("mrem", [P, 16])
        mparts = sb("mparts", [P, 2, 48], BF16)
        mrow = sb("mrow", [48, P], BF16)
        SH2 = sb("SH2", [P, 8 * T])
        oall = SH2[:, 0:1152].rearrange("p (g j d) -> p g j d", j=HF, d=HD0 + 1)
        rs = SH2[:, 1152:1280].rearrange("p (g j) -> p g j", j=HF)
        od = SH2[:, 1280:2304].rearrange("p (u g h d) -> p u g h d", u=2, h=2, d=HD0)
        rms = SH2[:, 2304:2432].rearrange("p (u g) -> p u g", u=2)
        on = SH2[:, 2432:2944].rearrange("p (d h q) -> p d h q", h=H0, q=NT)
        q_sc = sb("q_sc", [P, 2, 88])
        hid = PROB[:, 0:1408].rearrange("p (t n) -> p t n", t=NT)
        hact = PROB[:, 1408:2816].rearrange("p (t n) -> p t n", t=NT)
        hT = PROB[:, 2816:4352].rearrange("p (t c n) -> p t c n", t=NT, c=3)
        qa, qn, qt_ = (PROB[:, 4352 + 1408 * i:4352 + 1408 * (i + 1)] for i in range(3))
        w_in = PROB[:, 0:1120]
        xq = PROB[:, 8576:9088].rearrange("p (t n) -> p t n", t=NT)
        k1 = KPAD[:, 0:8192].bitcast(F32).rearrange("p (g h n) -> p g h n", g=NKV, h=2)
        qT = SH2[:, :].rearrange("p (c n) -> p c n", c=8)
        oT = SH[:, 0:4096].rearrange("p (c n) -> p c n", c=8)
        ropeT = SH[:, 4096:6144].rearrange("p (s u n) -> p s u n", s=2, u=2)
        v1 = KPAD[:, 8192:10240].bitcast(F32).rearrange("p (t n) -> p t n", t=NT)
        m1row = sb("m1row", [3, 2, 4 * T], BF16)
        rsum = KPAD[:, 10240:11264].bitcast(F32)
        hE = qT[:, :, :].rearrange("p (s f) n -> p s f n", s=2)
        xnT = SH[:, 0:512]
        acc = SH[:, 512:1024].rearrange("p (t n) -> p t n", t=NT)
        rt = sb("rt", [P, 6, NT, NE])
        rs1 = sb("rs1", [P, 4, NT])
        ohT = sb("ohT", [NE, T])

        ps = ctx.enter_context(nc.psum_tensor("ps", [P, 8, 512], F32))

        weights_in = sem("weights_in")
        setup_act = sem("setup_act")
        setup_pe = sem("setup_pe")
        setup_dve = sem("setup_dve")
        setup_pool = sem("setup_pool")
        x_in = sig("x_in")
        parts_out = sig("parts_out")
        terms_in = sig("terms_in")
        max0_in = sig("max0_in")
        max1_in = sig("max1_in")
        row_out = sig("row_out")
        tpose_x = sig("tpose_x")
        xT_ready = sig("xT_ready")
        proj0 = sig("proj0")
        hi_ready = sig("hi_ready")
        rem_ready = sig("rem_ready")
        parts_ready = sig("parts_ready")
        qzero = sig("qzero")
        v0_ready = sig("v0_ready")
        kpad_ready = sig("kpad_ready")
        s0_ready = sig("s0_ready")
        exp0_done = sig("exp0_done")
        a0_ready = sig("a0_ready")
        max0_done = sig("max0_done")
        mparts_ready = sig("mparts_ready")
        mtp_ready = sig("mtp_ready")
        mrow_ready = sig("mrow_ready")
        av0_done = sig("av0_done")
        o0_out = sig("o0_out")
        o0_tp = sig("o0_tp")
        o0_kept = sig("o0_kept")
        ms_ready = sig("ms_ready")
        rms_ready = sig("rms_ready")
        on_ready = sig("on_ready")
        y_ready = sig("y_ready")
        var_ready = sig("var_ready")
        std_ready = sig("std_ready")
        ln_done = sig("ln_done")
        xq_ready = sig("xq_ready")
        gu_ready = sig("gu_ready")
        silu_done = sig("silu_done")
        hid_done = sig("hid_done")
        hq_ready = sig("hq_ready")
        htp_ready = sig("htp_ready")
        hT_ready = sig("hT_ready")
        proj1 = sig("proj1")
        rope_ready = sig("rope_ready")
        qk_ready = sig("qk_ready")
        v1_ready = sig("v1_ready")
        s1_ready = sig("s1_ready")
        exp1_done = sig("exp1_done")
        a1_ready = sig("a1_ready")
        max1_done = sig("max1_done")
        av1_done = sig("av1_done")
        oT_ready = sig("oT_ready")
        logits_ready = sig("logits_ready")
        lc_ready = sig("lc_ready")
        le_ready = sig("le_ready")
        oh_ready = sig("oh_ready")
        ohT_ps = sig("ohT_ps")
        ohT_ready = sig("ohT_ready")
        up_ready = sig("up_ready")
        relu_act = sig("relu_act")
        relu_dve = sig("relu_dve")
        down_ready = sig("down_ready")
        comb_done = sig("comb_done")
        bias2_ready = sig("bias2_ready")
        act_order = sig("act_order")
        dve_order = sig("dve_order")
        pool_order = sig("pool_order")

        row_ended = ctx.enter_context(nc.semaphore("row_ended"))
        row_opened = [ctx.enter_context(nc.semaphore(f"row_opened_{e}")) for e in ("pool", "dve", "act", "pe")]
        n_loads, lam_ready, setup_count = [0], [0], [0]

        block = ctx.enter_context(nc.Block())

        def bcast(row, n):
            return bass.AP(tensor=row.tensor, offset=row.offset, ap=[[0, P], [1, n]])

        @block.sync
        def _(sp):
            loads = [
                (cst[:, :], const), (rope_sb[:, :, :], rope), (wqkv_sb[:, :], w_qkv), (wo0_sb[:, :], wo),
                (lam_in[:, 0], bcast(lq1, HD0)), (lam_in[:, 1], bcast(lk1, HD0)),
                (lam_in[:, 2], bcast(lq2, HD0)), (lam_in[:, 3], bcast(lk2, HD0)),
                (nw_sb[:, :], bass.AP(tensor=norm_w.tensor, offset=norm_w.offset, ap=[[0, P], [1, P]])),
                (w_in[:, 768:1120], w_down),
                (wq_sb[:, 0], Wq), (wk_in[:, :], Wk), (wv_sb[:, :], Wv),
                (wo1_sb[:, :, :], Wo.rearrange("(c p) n -> p c n", p=P)),
                (bv_sb[:, :], bcast(bv, NKV * D1)), (bo_sb[:, :], bcast(bo, E)),
                (wr_sb[:, :], Wr), (br_sb[:, :], bcast(br, NE)),
                (lng[:, 0:1], ln_g.rearrange("(p a) -> p a", a=1)), (lng[:, 1:2], ln_b.rearrange("(p a) -> p a", a=1)),
                (w1_sb[:, :, :], W1.rearrange("e d f -> d e f")),
                (w2_sb[:, :, :, :], W2.rearrange("e (c p) d -> p e c d", p=P)),
                (b2_sb[:, :], b2),
            ]
            for i, w in enumerate((w_gate, w_up)):
                loads.append((w_in[:, 384 * i:384 * i + 256].rearrange("p (c n) -> p c n", c=2),
                              w[0:256, :].rearrange("(c p) n -> p c n", p=P)))
                loads.append((w_in[0:96, 384 * i + 256:384 * i + 384], w[256:FF0, :]))
            for c in range(FF1 // P):
                loads.append((b1_sb[:, :, c], b1.rearrange("e (c p) -> c p e", p=P)[c]))
            bq_rows = bq.rearrange("(c p) -> p c", p=P)
            bk_rows = bk.rearrange("(g p) -> p g", p=D1)
            loads.append((bqk[:, 0, 0:8], bq_rows))
            for h in range(2):
                loads.append((bqk[64 * h:64 * h + 64, 0, 8:12], bk_rows))
                for u in range(2):
                    to, of_ = 64 * h + 32 * u, 64 * h + 32 * (1 - u)
                    loads.append((bqk[to:to + 32, 1, 0:8], bq_rows[of_:of_ + 32, :]))
                    loads.append((bqk[to:to + 32, 1, 8:12], bk_rows[32 * (1 - u):32 * (1 - u) + 32, :]))
            sp.wait_ge(setup_pool, 1)
            for dst, src in loads:
                sp.dma_start(dst, src, allow_slow_non_contiguous=True).then_inc(weights_in, 16)
            n_loads[0] = len(loads)
            with sp.Fori(0, BATCH) as row:
                sp.dma_start(X[:, :, :], x_rows[bass.ds(row, 1)].rearrange("a p t e -> (a p) t e")).then_inc(x_in, 16)
                for c in range(2):
                    sp.wait_ge(parts_ready, c + 1)
                    sp.dma_start(parts_dram[c].rearrange("s p n -> p s n"), split[:, c]).then_inc(parts_out, 16)
                sp.wait_ge(parts_out, 32)
                sp.wait_ge(qzero, 1)
                for c, (dst, part) in enumerate(((kst, K_PART), (qst, Q_PART))):
                    for t in range(NTERM):
                        src = parts_dram[1 - c, part[t]].rearrange("(g r) n -> r g n", g=NG)
                        sp.dma_start(dst[16 * t:16 * t + 16], src).then_inc(terms_in, 16)
                for g in range(NG):
                    sp.wait_ge(mrow_ready, g + 1)
                    sp.dma_start(qst[M_ROW:M_ROW + 12, g, :], mrow[:, :]).then_inc(max0_in, 16)
                    sp.wait_ge(max0_in, 16 * (g + 1))
                for g in range(NKV):
                    sp.wait_ge(mrow_ready, NG + g + 1)
                    sp.dma_start(m1row[:, g % 2, :], mrow[:, :]).then_inc(max1_in, 16)
                    sp.wait_ge(max1_in, 16 * (g + 1))
                sp.wait_ge(ln_done, 5)
                sp.dma_start(out_rows[bass.ds(row, 1)].rearrange("a p t e -> (a p) t e"), X[:, :, :]).then_inc(row_out, 16)
                sp.wait_ge(row_out, 16)
                sp.wait_ge(row_ended, len(row_opened))
                sp.sem_clear(row_ended)
                for s in row_signals:
                    sp.sem_clear(s)
                for opened in row_opened:
                    sp.sem_inc(opened, 1)

        @block.gpsimd
        def _(pool):
            pool.memset(w_in, 0.0).then_inc(setup_pool, 1)
            pool.memset(v0[:, :, :, :], 0.0).then_inc(setup_pool, 1)
            pool.memset(ones[:, :], 1.0).then_inc(setup_pool, 1)
            pool.memset(ones3[:, :], 1.0).then_inc(setup_pool, 1)
            pool.memset(eps[:, 0:1], LN_EPS).then_inc(setup_pool, 1)
            pool.memset(eps[:, 1:2], RMS_EPS).then_inc(setup_pool, 1)
            pool.wait_ge(setup_pool, 2)
            pool.memset(v0[:, :, :, HD0:HD0 + 1], 1.0).then_inc(setup_pool, 1)
            with pool.Fori(0, BATCH) as row:
                own = [0]

                def step(ins):
                    ins.then_inc(pool_order, 1)
                    own[0] += 1

                def settle():
                    pool.wait_ge(pool_order, own[0])

                for c in range(2):
                    pool.wait_ge(rem_ready, c + 1)
                    step(pool.tensor_copy(split[:, c, 1], rem[:, c]))
                    settle()
                    pool.tensor_tensor(split[:, c, 2], rem[:, c], split[:, c, 1], ALU.subtract).then_inc(parts_ready, 1)
                pool.wait_ge(parts_ready, 2)
                step(pool.memset(qst[96:128], 0.0))
                step(pool.memset(kst[96:128], 0.0))
                settle()
                pool.memset(kst[M_ROW:M_ROW + 12], 1.0).then_inc(qzero, 1)

                def max_parts(i, mdone, upto):
                    pool.wait_ge(mdone, upto)
                    if i:
                        pool.wait_ge(mparts_ready, i)
                    else:
                        pool.wait_ge(qzero, 1)
                    if i >= 2:
                        pool.wait_ge(mtp_ready, i - 1)
                    m = mx[:, i % 2]
                    part = [mparts[:, i % 2, 16 * s:16 * s + 16] for s in range(3)]
                    step(pool.tensor_copy(part[0], m))
                    settle()
                    step(pool.tensor_tensor(mrem[:, :], m, part[0], ALU.subtract))
                    settle()
                    step(pool.tensor_copy(part[1], mrem[:, :]))
                    settle()
                    pool.tensor_tensor(part[2], mrem[:, :], part[1], ALU.subtract).then_inc(mparts_ready, 1)

                for g in range(NG):
                    max_parts(g, max0_done, 16 * (g + 1))
                for c in range(12):
                    pool.wait_ge(rope_ready, 2 * (c + 1))
                    a, r = ropeT[:, c % 2, 0], ropeT[:, c % 2, 1]
                    if c < 8:
                        pool.tensor_tensor(qT[:, c], a, r, ALU.add).then_inc(qk_ready, 1)
                    else:
                        g = c - 8
                        if c == 8:
                            pool.wait_ge(qk_ready, 8)
                            step(pool.memset(k1[0:64, :, 1], 0.0))
                            settle()
                            step(pool.memset(k1[64:128, :, 0], 0.0))
                            settle()
                        else:
                            pool.wait_ge(qk_ready, c)
                        step(pool.tensor_tensor(k1[0:64, g, 0], a[0:64], r[0:64], ALU.add))
                        settle()
                        pool.tensor_tensor(k1[64:128, g, 1], a[64:128], r[64:128], ALU.add).then_inc(qk_ready, 1)
                for g in range(NKV):
                    max_parts(NG + g, max1_done, 16 * (g + 1))
                pool.wait_ge(mparts_ready, NG + NKV)
                pool.sem_inc(row_ended, 1)
                pool.wait_ge(row_opened[0], 1)
                pool.sem_clear(row_opened[0])

        @block.vector
        def _(dve):
            own = [0]

            def setup(ins):
                ins.then_inc(setup_dve, 1)
                own[0] += 1

            def settle():
                dve.wait_ge(setup_dve, own[0])

            def quantise(src, n, step, settle):
                nb = n // QB
                blk = lambda t: t.rearrange("p (b q) -> p b q", q=QB)
                s, r = q_sc[:, 0, 0:nb], q_sc[:, 1, 0:nb]
                wide = lambda t: t.rearrange("p (b a) -> p b a", a=1).broadcast_to([P, nb, QB])
                a, c, t = qa[:, 0:n], qn[:, 0:n], qt_[:, 0:n]
                step(dve.tensor_reduce(s, blk(src), AX, ALU.max, apply_absolute_value=True)); settle()
                step(dve.tensor_scalar(s, s, 1.0 / 6.0, 1e-12, ALU.mult, ALU.max)); settle()
                step(dve.reciprocal(r, s)); settle()
                step(dve.tensor_tensor(blk(a), blk(src), wide(r), ALU.mult)); settle()
                step(dve.scalar_tensor_tensor(a, a, -1.0, a, ALU.mult, ALU.max)); settle()
                step(dve.tensor_scalar(t, a, 5.0, 2.0, ALU.is_gt, ALU.mult))
                step(dve.tensor_scalar(c, a, 0.25, None, ALU.is_gt)); settle()
                for lim in (3.5, 2.5):
                    step(dve.scalar_tensor_tensor(t, a, lim, t, ALU.is_gt, ALU.add)); settle()
                for lim in (0.75, 1.25, 1.75):
                    step(dve.scalar_tensor_tensor(c, a, lim, c, ALU.is_gt, ALU.add)); settle()
                step(dve.scalar_tensor_tensor(c, t, 2.0, c, ALU.mult, ALU.add))
                step(dve.tensor_scalar(s, s, 0.5, None, ALU.mult)); settle()
                step(dve.tensor_tensor(blk(a), blk(c), wide(s), ALU.mult)); settle()
                step(dve.scalar_tensor_tensor(a.bitcast(U32), src.bitcast(U32), SIGN, a.bitcast(U32),
                                              ALU.bitwise_and, ALU.bitwise_or))

            dve.wait_ge(setup_pool, 7)
            dve.wait_ge(weights_in, 16 * n_loads[0])
            setup(dve.tensor_copy(bmask[:, :, :], cst[:, 0:3 * P].rearrange("p (a n) -> p a n", a=3)))
            for i in range(2):
                setup(dve.tensor_tensor(lam_w[:, i], lam_in[:, 2 * i], lam_in[:, 2 * i + 1], ALU.mult))
            settle()
            setup(dve.tensor_reduce(lam_s[:, 0:2], lam_w[:, :, :], AX, ALU.add))
            settle()
            lam_at = own[0]
            dve.wait_ge(setup_act, 1)
            setup(dve.scalar_tensor_tensor(lam[:, :], lam_s[:, 2:3], LAMBDA_INIT, lam_s[:, 3:4], ALU.add, ALU.subtract))
            setup(dve.tensor_scalar(nw_sb[:, :], nw_sb[:, :], 1.0 - LAMBDA_INIT, None, ALU.mult))
            wq_h = wq_sb[:, :, :].rearrange("p u (h a d) -> p u h a d", a=2, d=D1 // 2)
            setup(dve.tensor_scalar(wq_h[:, 1, :, 0], wq_h[:, 0, :, 1], -1.0, None, ALU.mult))
            setup(dve.tensor_copy(wq_h[:, 1, :, 1], wq_h[:, 0, :, 0]))
            wk_h = wk_in[:, :].rearrange("p (g a d) -> p g a d", a=2, d=D1 // 2)
            for i in range(2):
                to = wk_sb[:, :, :, i, :].rearrange("p u g (a d) -> p u g a d", a=2)
                setup(dve.tensor_copy(to[:, 0], wk_h))
                setup(dve.tensor_scalar(to[:, 1, :, 0], wk_h[:, :, 1], -1.0, None, ALU.mult))
                setup(dve.tensor_copy(to[:, 1, :, 1], wk_h[:, :, 0]))
            setup(dve.tensor_scalar(bqk[:, 1], bqk[:, 1], rot_sign, None, ALU.mult))
            quantise(w_in, 1120, setup, settle)
            settle()
            setup_total = own[0]
            lam_ready[0], setup_count[0] = lam_at, setup_total

            with dve.Fori(0, BATCH) as row:
                own = [0]

                def step(ins):
                    ins.then_inc(dve_order, 1)
                    own[0] += 1

                def settle():
                    dve.wait_ge(dve_order, own[0])


                def layer_norm(i, base, extra=()):
                    step(dve.tensor_tensor(Z[:, :, :], X[:, :, :], base, ALU.add)); settle()
                    for e in extra:
                        step(dve.tensor_tensor(Z[:, :, :], Z[:, :, :], e, ALU.add)); settle()
                    centre_and_scale(i, Z[:, :, :], X[:, :, :])

                def centre_and_scale(i, src, dst):
                    wide = lambda t: t.rearrange("p (t a) -> p t a", a=1).broadcast_to([P, NT, E])
                    step(dve.tensor_reduce(st[:, 0], src, AX, ALU.add)); settle()
                    step(dve.tensor_scalar(st[:, 0], st[:, 0], -1.0 / E, None, ALU.mult)); settle()
                    step(dve.tensor_tensor(Z[:, :, :], src, wide(st[:, 0]), ALU.add)); settle()
                    step(dve.tensor_tensor(ZS[:, :, :], Z[:, :, :], Z[:, :, :], ALU.mult)); settle()
                    dve.tensor_reduce(st[:, 1], ZS[:, :, :], AX, ALU.add).then_inc(var_ready, 1)
                    dve.wait_ge(std_ready, i + 1)
                    step(dve.reciprocal(st[:, 3], st[:, 2])); settle()
                    dve.tensor_tensor(dst, Z[:, :, :], wide(st[:, 3]), ALU.mult).then_inc(ln_done, 1)

                tiles = lambda bank: ps[:, bank, :].rearrange("p (t n) -> p t n", t=NT)

                for c in range(2):
                    dve.wait_ge(hi_ready, c + 1)
                    dve.tensor_tensor(rem[:, c], ps[:, c, :], split[:, c, 0], ALU.subtract).then_inc(rem_ready, 1)
                dve.wait_ge(proj0, 3)
                dve.tensor_copy(v0[:, :, :, 0:HD0], ps[:, 2, :].rearrange("p (t h d) -> p t h d", t=NT, h=H0)).then_inc(v0_ready, 1)
                dve.wait_ge(terms_in, 16 * 12)
                for j in range(HF):
                    dve.tensor_scalar(kpad[:, :, j, :], kst, jmask[:, j:j + 1], None, ALU.mult).then_inc(kpad_ready, 1)

                for s in range(-4, 18):
                    a = s + 4
                    for c in range(4):
                        if a < 16:
                            ga = a // 2
                            for u in range(2):
                                r = 8 * a + 2 * c + u
                                dve.wait_ge(a0_ready, r + 1)
                                if r % 16 == 0 and ga >= 2:
                                    dve.wait_ge(mparts_ready, ga - 1)
                                dve.tensor_reduce(mx[:, ga % 2, r % 16:r % 16 + 1], ps[:, 4 + r % 2, :], AX, ALU.max,
                                                       negate=True).then_inc(max0_done, 1)
                        if c == 1 and s % 2 == 0 and -2 <= s <= 12:
                            g = s // 2 + 1
                            dve.wait_ge(mtp_ready, g + 1)
                            dve.wait_ge(max0_in, 16 * g)
                            dve.tensor_copy(mrow[:, :], ps[:, 7, :].bitcast(BF16)[0:48, 0:P]).then_inc(mrow_ready, 1)
                        if c == 1 and s % 2 == 1 and s >= 3:
                            g = (s - 3) // 2
                            dve.wait_ge(o0_tp, g + 1)
                            src = ps[:, 7, :].rearrange("p (q j r) -> p q j r", q=NT, j=HF)[:, :, :, 0:HD0 + 1]
                            dve.tensor_copy(oall[:, NT * g:NT * g + NT], src).then_inc(o0_kept, 1)
                dve.wait_ge(o0_kept, NG)
                step(dve.reciprocal(rs[:, :, :], oall[:, :, :, HD0])); settle()
                step(dve.tensor_scalar(rs[:, :, 1::2], rs[:, :, 1::2], lam[:, 0:1], None, ALU.mult)); settle()
                for u in range(2):
                    w = rs[:, :, u::2].rearrange("p g (h a) -> p g h a", a=1).broadcast_to([P, NG * NT, 2, HD0])
                    step(dve.tensor_tensor(od[:, u], oall[:, :, u::2, 0:HD0], w, ALU.mult))
                settle()
                step(dve.tensor_tensor(od[:, 0], od[:, 0], od[:, 1], ALU.subtract)); settle()
                step(dve.tensor_tensor(od[:, 1], od[:, 0], od[:, 0], ALU.mult)); settle()
                dve.tensor_reduce(rms[:, 0], od[:, 1].rearrange("p g h d -> p (g h) d"), AX, ALU.add).then_inc(ms_ready, 1)
                dve.wait_ge(rms_ready, 1)
                step(dve.reciprocal(rms[:, 0], rms[:, 1])); settle()
                w = rms[:, 0].rearrange("p (g a) -> p g a", a=1).broadcast_to([P, NG * NT * 2, HD0])
                o0 = od[:, 0].rearrange("p g h d -> p (g h) d")
                step(dve.tensor_tensor(o0, o0, w, ALU.mult)); settle()
                o4 = od[:, 0].rearrange("p (g q) h d -> p q g h d", q=NT)
                for q in range(NT):
                    dst = on[:, :, :, q].rearrange("p d (g h) -> p g h d", h=2)
                    dve.tensor_tensor(dst, o4[:, q], nw_sb[:, :].rearrange("p (g h d) -> p g h d", h=2, d=HD0), ALU.mult).then_inc(on_ready, 1)
                dve.wait_ge(y_ready, 1)
                layer_norm(0, tiles(4))

                dve.wait_ge(ln_done, 1)
                quantise(X[:, :, :].rearrange("p t n -> p (t n)"), T, step, settle)
                settle()
                dve.tensor_copy(xq.rearrange("p t n -> p (t n)"), qa[:, 0:T]).then_inc(xq_ready, 1)
                for t in range(NT):
                    dve.wait_ge(silu_done, t + 1)
                    dve.tensor_tensor(hid[:, t], hact[:, t], ps[:, 2 * (t % 2) + 1, 0:FF0], ALU.mult).then_inc(hid_done, 1)
                dve.wait_ge(hid_done, NT)
                quantise(PROB[:, 0:1408], 1408, step, settle)
                settle()
                dve.sem_inc(hq_ready, 1)
                dve.wait_ge(y_ready, 2)
                layer_norm(1, tiles(6))

                for c in range(12):
                    dve.wait_ge(proj1, c + 1)
                    if c >= 2:
                        dve.wait_ge(qk_ready, c - 1)
                    for u in range(2):
                        dve.scalar_tensor_tensor(ropeT[:, c % 2, u], ps[:, 2 * (c % 2) + u, :], bqk[:, u, c:c + 1],
                                                      rope_sb[:, u], ALU.add, ALU.mult).then_inc(rope_ready, 1)
                bvw = bv_sb[:, :].rearrange("p (a n) -> p a n", a=1).broadcast_to([P, 2, NKV * D1])
                for i in range(2):
                    dve.wait_ge(proj1, 13 + i)
                    dve.tensor_tensor(v1[:, 2 * i:2 * i + 2], ps[:, 4 + i, :].rearrange("p (t n) -> p t n", t=2),
                                           bvw, ALU.add).then_inc(v1_ready, 1)

                def normalise(i):
                    dve.wait_ge(av1_done, i + 1)
                    step(dve.reciprocal(rsum, ps[:, 7, :])); settle()
                    dve.tensor_tensor(oT[:, i], ps[:, 6, :], rsum, ALU.mult).then_inc(oT_ready, 1)
                    dve.wait_ge(oT_ready, i + 1)

                for s in range(-1, NKV + 1):
                    if 0 <= s < NKV:
                        dve.wait_ge(mtp_ready, NG + s + 1)
                        if s == 0:
                            dve.wait_ge(max0_in, 16 * NG)
                        else:
                            dve.wait_ge(max1_in, 16 * s)
                        dve.tensor_copy(mrow[:, :], ps[:, 4, :].bitcast(BF16)[0:48, 0:P]).then_inc(mrow_ready, 1)
                    if s >= 1:
                        normalise(2 * (s - 1))
                        normalise(2 * (s - 1) + 1)
                    if s + 1 < NKV:
                        ga = s + 1
                        dve.wait_ge(mparts_ready, NG + ga - 1)
                        for i in range(16):
                            r = 16 * ga + i
                            dve.wait_ge(a1_ready, r + 1)
                            w = P * (i % 4 + 1)
                            dve.tensor_reduce(mx[:, ga % 2, i:i + 1], ps[:, 4 + r % 2, 0:w], AX, ALU.max,
                                                   negate=True).then_inc(max1_done, 1)
                dve.wait_ge(y_ready, 3)
                bow = bo_sb[:, :].rearrange("p (a n) -> p a n", a=1).broadcast_to([P, NT, E])
                layer_norm(2, tiles(4), (bow,))

                L, EX, IS, OH, OG = (rt[:, i] for i in range(5))
                top, se, gate, mw = (rs1[:, i] for i in range(4))
                each = lambda t: t.rearrange("p (t a) -> p t a", a=1).broadcast_to([P, NT, NE])
                every = lambda t: t.rearrange("p (a n) -> p a n", a=1).broadcast_to([P, NT, NE])
                dve.wait_ge(logits_ready, 1)
                step(dve.tensor_tensor(L, ps[:, 5, 0:NT * NE].rearrange("p (t n) -> p t n", t=NT), every(br_sb[:, :]), ALU.add)); settle()
                step(dve.tensor_reduce(top, L, AX, ALU.max)); settle()
                step(dve.tensor_tensor(IS, L, each(top), ALU.is_equal))
                dve.tensor_tensor(OG, L, each(top), ALU.subtract).then_inc(lc_ready, 1); settle()
                step(dve.tensor_tensor(IS, IS, every(rank), ALU.mult)); settle()
                step(dve.tensor_reduce(mw, IS, AX, ALU.max)); settle()
                step(dve.tensor_tensor(OH, IS, each(mw), ALU.is_equal))
                dve.wait_ge(le_ready, 1)
                step(dve.tensor_reduce(se, EX, AX, ALU.add)); settle()
                step(dve.reciprocal(gate, se)); settle()
                dve.tensor_tensor(OG, OH, each(gate), ALU.mult).then_inc(oh_ready, 1)
                centre_and_scale(3, X[:, :, :], Z[:, :, :])
                dve.wait_ge(tpose_x, 5)
                dve.tensor_scalar(xnT, ps[:, 7, :], lng[:, 0:1], lng[:, 1:2], ALU.mult, ALU.add).then_inc(xT_ready, 1)
                dve.wait_ge(ohT_ps, 1)
                dve.tensor_copy(ohT[:, :], ps[0:NE, 5, :]).then_inc(ohT_ready, 1)

                def combine(e):
                    dve.wait_ge(down_ready, e + 1)
                    for t in range(NT):
                        src, g = ps[:, 4 + e % 2, t * P:(t + 1) * P], OG[:, t, e:e + 1]
                        if e == 0:
                            ins = dve.tensor_scalar(acc[:, t], src, g, None, ALU.mult)
                        else:
                            ins = dve.scalar_tensor_tensor(acc[:, t], src, g, acc[:, t], ALU.mult, ALU.add)
                        ins.then_inc(comb_done, 1)
                    dve.wait_ge(comb_done, NT * (e + 1))

                for e in range(NE):
                    for f in (1, 3):
                        dve.wait_ge(up_ready, 4 * e + f + 1)
                        if e >= 2:
                            dve.wait_ge(down_ready, e - 1)
                        dve.tensor_scalar(hE[:, e % 2, f], ps[:, f, :], b1_sb[:, e, f:f + 1], 0.0, ALU.add, ALU.max).then_inc(relu_dve, 1)
                    if e >= 1:
                        combine(e - 1)
                combine(NE - 1)
                dve.wait_ge(bias2_ready, 1)
                layer_norm(4, tiles(6), (acc,))
                dve.wait_ge(ln_done, 5)
                dve.sem_inc(row_ended, 1)
                dve.wait_ge(row_opened[1], 1)
                dve.sem_clear(row_opened[1])

        @block.scalar
        def _(act):
            act.wait_ge(setup_dve, lam_ready[0])
            act.activation(lam_s[:, 2:4], lam_s[:, 0:2], ACT.Exp).then_inc(setup_act, 1)
            for i in range(3):
                act.wait_ge(setup_pe, i + 1)
                if i < 2:
                    act.copy(wgT[:, i, :], ps[:, i, 0:FF0]).then_inc(setup_act, 1)
                else:
                    act.copy(wdT[:, 0:2, :], ps[:, 2, 0:256].rearrange("p (c n) -> p c n", c=2)).then_inc(setup_act, 1)
                    act.copy(wdT[0:96, 2, :], ps[0:96, 2, 256:384]).then_inc(setup_act, 1)
            with act.Fori(0, BATCH) as row:

                def copy_xT(i):
                    act.wait_ge(tpose_x, i + 1)
                    act.copy(xT[:, :], ps[:, 7, :]).then_inc(xT_ready, 1)

                def std(i):
                    act.wait_ge(var_ready, i + 1)
                    act.activation(st[:, 2], st[:, 1], ACT.Sqrt, bias=eps[:, 0:1], scale=1.0 / E).then_inc(std_ready, 1)

                def keep_o(g):
                    act.wait_ge(av0_done, 2 * (g + 1))
                    act.wait_ge(o0_tp, g)
                    act.copy(osb, ps[:, 6, :]).then_inc(o0_out, 1)

                copy_xT(0)
                for c in range(2):
                    act.wait_ge(proj0, c + 1)
                    act.copy(split[:, c, 0], ps[:, c, :]).then_inc(hi_ready, 1)
                for n in range(16):
                    for c in range(HF):
                        q = 4 * n + c
                        act.wait_ge(s0_ready, q + 1)
                        if c == 0 and n >= 2:
                            act.wait_ge(av0_done, n - 1)
                        act.activation(prob0[:, n % 2, c], ps[:, 2 * (q % 2):2 * (q % 2) + 2, :], ACT.Exp,
                                            scale=float(HD0) ** -0.5).then_inc(exp0_done, 1)
                    if n % 2 == 0 and n >= 2:
                        keep_o(n // 2 - 1)
                keep_o(NG - 1)
                act.wait_ge(ms_ready, 1)
                act.activation(rms[:, 1], rms[:, 0], ACT.Sqrt, bias=eps[:, 1:2], scale=1.0 / HD0).then_inc(rms_ready, 1)
                std(0)
                copy_xT(1)
                for t in range(NT):
                    act.wait_ge(gu_ready, t + 1)
                    act.activation(hact[:, t], ps[:, 2 * (t % 2), 0:FF0], ACT.Silu).then_inc(silu_done, 1)
                for t in range(NT):
                    act.wait_ge(htp_ready, t + 1)
                    bank = 4 + t % 2
                    act.copy(hT[:, t, 0:2, :], ps[:, bank, 0:256].rearrange("p (c n) -> p c n", c=2)).then_inc(hT_ready, 1)
                    act.copy(hT[0:96, t, 2, :], ps[0:96, bank, 256:384]).then_inc(hT_ready, 1)
                std(1)
                copy_xT(2)
                for s in range(NKV):
                    for c in range(5):
                        q = 5 * s + c
                        act.wait_ge(s1_ready, q + 1)
                        if c == 0 and s >= 2:
                            act.wait_ge(av1_done, 2 * (s - 1))
                        src = ps[:, 2 * (q % 2):2 * (q % 2) + 2, :]
                        if c < 4:
                            dst = prob1[:, s % 2, c, 0:1024].rearrange("p (k n) -> p k n", k=2)
                        else:
                            dst, src = prob1[:, s % 2, :, 1024:PW], src.rearrange("p k (h n) -> p (k h) n", h=2)
                        act.activation(dst, src, ACT.Exp, scale=float(D1) ** -0.5).then_inc(exp1_done, 1)
                std(2)
                copy_xT(3)
                act.wait_ge(lc_ready, 1)
                act.activation(rt[:, 1], rt[:, 4], ACT.Exp).then_inc(le_ready, 1)
                std(3)
                for e in range(NE):
                    for f in (0, 2):
                        act.wait_ge(up_ready, 4 * e + f + 1)
                        if e >= 2:
                            act.wait_ge(down_ready, e - 1)
                        act.activation(hE[:, e % 2, f], ps[:, f, :], ACT.Relu, bias=b1_sb[:, e, f:f + 1]).then_inc(relu_act, 1)
                std(4)
                act.wait_ge(std_ready, 5)
                act.sem_inc(row_ended, 1)
                act.wait_ge(row_opened[2], 1)
                act.sem_clear(row_opened[2])

        @block.tensor
        def _(pe):
            pe.wait_ge(setup_dve, setup_count[0])
            for i in range(2):
                for c, w in enumerate(FCH):
                    ins = pe.transpose(ps[:, i, P * c:P * c + w], qa[0:w, 384 * i + P * c:384 * i + P * (c + 1)], ident[0:w, 0:w])
                ins.then_inc(setup_pe, 1)
            for c, w in enumerate(FCH):
                ins = pe.transpose(ps[0:w, 2, P * c:P * (c + 1)], qa[:, 768 + P * c:768 + P * c + w], ident)
            ins.then_inc(setup_pe, 1)
            pe.wait_ge(setup_act, 5)
            with pe.Fori(0, BATCH) as row:

                def transpose_tiles(src):
                    for t in range(NT):
                        ins = pe.transpose(ps[:, 7, P * t:P * (t + 1)], src[:, t, :], ident)
                    ins.then_inc(tpose_x, 1)

                pe.wait_ge(x_in, 16)
                transpose_tiles(X)
                pe.wait_ge(xT_ready, 1)
                for c in range(2):
                    pe.matmul(ps[:, c, :], wqkv_sb[:, c * E:(c + 1) * E], xT[:, :], start=True, stop=True).then_inc(proj0, 1)
                for t in range(NT):
                    ins = pe.matmul(ps[:, 2, P * t:P * (t + 1)], xT[:, P * t:P * (t + 1)], wqkv_sb[:, 2 * E:], start=True, stop=True)
                ins.then_inc(proj0, 1)
                pe.wait_ge(kpad_ready, HF)
                pe.wait_ge(v0_ready, 1)
                pe.wait_ge(rem_ready, 2)
                for s in range(-4, 18):
                    a, n, m = s + 4, s, s - 1
                    for c in range(4):
                        if 0 <= n < 16:
                            q, g = 4 * n + c, n // 2
                            if q >= 2:
                                pe.wait_ge(exp0_done, q - 1)
                            if c == 0 and n % 2 == 0:
                                pe.wait_ge(max0_in, 16 * (g + 1))
                            for k in range(2):
                                kt = 2 * (n % 2) + k
                                ins = pe.matmul(ps[:, 2 * (q % 2) + k, :], kpad[:, g, c, P * kt:P * (kt + 1)], qst[:, g, :],
                                                start=True, stop=True)
                            ins.then_inc(s0_ready, 1)
                        if a < 16:
                            for u in range(2):
                                r = 8 * a + 2 * c + u
                                j, qt = r % 16 // 4, r % 4
                                if r >= 2:
                                    pe.wait_ge(max0_done, r - 1)
                                pe.matmul(ps[:, 4 + r % 2, :], qst[:, a // 2, P * qt:P * (qt + 1)], kpad[:, a // 2, j, :],
                                               start=True, stop=True).then_inc(a0_ready, 1)
                        if c == 1 and s % 2 == 0 and -2 <= s <= 12:
                            g = s // 2 + 1
                            pe.wait_ge(mparts_ready, g + 1)
                            if s >= 4:
                                pe.wait_ge(o0_kept, (s - 2) // 2)
                            pe.transpose(ps[:, 7, :].bitcast(BF16)[0:48, 0:P], mparts[:, g % 2], identb).then_inc(mtp_ready, 1)
                        if c == 1 and s % 2 == 1 and s >= 3:
                            g = (s - 3) // 2
                            pe.wait_ge(mrow_ready, min(NG, (s + 1) // 2 + 1))
                            pe.wait_ge(o0_kept, g)
                            pe.wait_ge(o0_out, g + 1)
                            for t in range(NT):
                                ins = pe.transpose(ps[:, 7, P * t:P * (t + 1)], osb[:, P * t:P * (t + 1)], ident)
                            ins.then_inc(o0_tp, 1)
                        if 0 <= m < 16 and c in (1, 2):
                            if c == 1:
                                pe.wait_ge(exp0_done, 4 * (m + 1))
                                if m % 2 == 0:
                                    pe.wait_ge(o0_out, m // 2)
                            kt = 2 * (m % 2) + c - 1
                            for j in range(HF):
                                ins = pe.matmul(ps[32 * j:32 * j + 32, 6, :], v0[:, kt, 2 * (m // 2) + j // 2, :],
                                                prob0[:, m % 2, j, c - 1, :], start=(kt == 0), stop=(kt == 3))
                            if c == 2:
                                ins.then_inc(av0_done, 1)
                pe.wait_ge(on_ready, NT)
                for t in range(NT):
                    ins = pe.matmul(ps[:, 4, P * t:P * (t + 1)], on[:, 2 * t:2 * t + 2].rearrange("p d h q -> p (d h q)"),
                                    wo0_sb[:, :], start=True, stop=True)
                ins.then_inc(y_ready, 1)

                pe.wait_ge(xq_ready, 1)
                transpose_tiles(xq)
                pe.wait_ge(xT_ready, 2)
                for t in range(NT):
                    if t >= 2:
                        pe.wait_ge(hid_done, t - 1)
                    for u in range(2):
                        ins = pe.matmul(ps[:, 2 * (t % 2) + u, 0:FF0], xT[:, P * t:P * (t + 1)], wgT[:, u, :], start=True, stop=True)
                    ins.then_inc(gu_ready, 1)
                pe.wait_ge(hq_ready, 1)
                for t in range(NT + 1):
                    if t < NT:
                        if t >= 2:
                            pe.wait_ge(hT_ready, 2 * (t - 1))
                        for c, w in enumerate(FCH):
                            ins = pe.transpose(ps[0:w, 4 + t % 2, P * c:P * (c + 1)], qa[:, FF0 * t + P * c:FF0 * t + P * c + w], ident)
                        ins.then_inc(htp_ready, 1)
                    if t >= 1:
                        pe.wait_ge(hT_ready, 2 * t)
                        for c, w in enumerate(FCH):
                            ins = pe.matmul(ps[:, 6, P * (t - 1):P * t], hT[0:w, t - 1, c, :], wdT[0:w, c, :],
                                            start=(c == 0), stop=(c == 2))
                ins.then_inc(y_ready, 1)

                pe.wait_ge(ln_done, 2)
                transpose_tiles(X)
                pe.wait_ge(xT_ready, 3)
                for c in range(12):
                    if c >= 2:
                        pe.wait_ge(rope_ready, 2 * (c - 1))
                    for u in range(2):
                        w = wq_sb[:, u, P * c:P * (c + 1)] if c < 8 else wk_sb[:, u, c - 8].rearrange("p a d -> p (a d)")
                        ins = pe.matmul(ps[:, 2 * (c % 2) + u, :], w, xT[:, :], start=True, stop=True)
                    ins.then_inc(proj1, 1)
                for i in range(2):
                    for k in range(2):
                        t = 2 * i + k
                        ins = pe.matmul(ps[:, 4 + i, 256 * k:256 * (k + 1)], xT[:, P * t:P * (t + 1)], wv_sb[:, :], start=True, stop=True)
                    ins.then_inc(proj1, 1)
                pe.wait_ge(qk_ready, 12)
                pe.wait_ge(v1_ready, 2)

                def scores1(g, h, kt, dst):
                    lo = P * kt
                    pe.matmul(dst, k1[:, g, h % 2, lo:lo + P], qT[:, 2 * g + h // 2, lo:], start=True, stop=False)
                    pe.matmul(dst[:, 0:P], identb, mask_kq, start=False, stop=False)
                    return pe.matmul(dst, ones3[:, :], m1row[:, g % 2, T * h + lo:T * (h + 1)], start=False, stop=True)

                def maxima1(g, i):
                    r, h, qt = 16 * g + i, i // 4, i % 4
                    w = P * (qt + 1)
                    if r >= 2:
                        pe.wait_ge(max1_done, r - 1)
                    if r % 16 == 0 and g >= 1:
                        pe.wait_ge(mrow_ready, NG + g)
                    dst = ps[:, 4 + r % 2, 0:w]
                    pe.matmul(dst, qT[:, 2 * g + h // 2, P * qt:P * (qt + 1)], k1[:, g, h % 2, 0:w], start=True, stop=False)
                    pe.matmul(dst[:, w - P:w], identb, mask_qk, start=False, stop=True).then_inc(a1_ready, 1)

                def values1(s, p_):
                    if p_ == 0:
                        pe.wait_ge(exp1_done, 5 * (s + 1))
                    pe.wait_ge(oT_ready, 2 * s + p_)
                    for bank in (6, 7):
                        for kt in range(4):
                            for h in range(2):
                                w = v1[:, kt, D1 * s:D1 * (s + 1)] if bank == 6 else ones[:, :]
                                ins = pe.matmul(ps[64 * h:64 * h + 64, bank, P * kt:T], w,
                                                prob1[:, s % 2, 2 * p_ + h, POFF[kt]:POFF[kt] + WID[kt]],
                                                start=(kt == 0), stop=(kt == 3))
                    ins.then_inc(av1_done, 1)

                for s in range(-1, NKV + 1):
                    if 0 <= s < NKV:
                        pe.wait_ge(mparts_ready, NG + s + 1)
                        pe.transpose(ps[:, 4, :].bitcast(BF16)[0:48, 0:P], mparts[:, (NG + s) % 2], identb).then_inc(mtp_ready, 1)
                    if s >= 1:
                        values1(s - 1, 0)
                        values1(s - 1, 1)
                    if 0 <= s < NKV:
                        pe.wait_ge(max1_in, 16 * (s + 1))
                    for c in range(5):
                        if 0 <= s < NKV:
                            q = 5 * s + c
                            if q >= 2:
                                pe.wait_ge(exp1_done, q - 1)
                            b0 = 2 * (q % 2)
                            if c < 4:
                                scores1(s, c, 0, ps[:, b0, :])
                                scores1(s, c, 1, ps[:, b0 + 1, 0:384])
                                ins = scores1(s, c, 3, ps[:, b0 + 1, 384:512])
                            else:
                                for h in range(4):
                                    ins = scores1(s, h, 2, ps[:, b0 + h // 2, 256 * (h % 2):256 * (h % 2) + 256])
                            ins.then_inc(s1_ready, 1)
                        if s + 1 < NKV and c < 4:
                            for i in range(4 * c, 4 * c + 4):
                                maxima1(s + 1, i)
                pe.wait_ge(oT_ready, 8)
                for t in range(NT):
                    for c in range(8):
                        ins = pe.matmul(ps[:, 4, P * t:P * (t + 1)], oT[:, c, P * t:P * (t + 1)], wo1_sb[:, c, :],
                                        start=(c == 0), stop=(c == 7))
                ins.then_inc(y_ready, 1)

                pe.wait_ge(ln_done, 3)
                transpose_tiles(X)
                pe.wait_ge(xT_ready, 4)
                for t in range(NT):
                    ins = pe.matmul(ps[:, 5, NE * t:NE * (t + 1)], xT[:, P * t:P * (t + 1)], wr_sb[:, :], start=True, stop=True)
                ins.then_inc(logits_ready, 1)
                pe.wait_ge(ln_done, 4)
                transpose_tiles(Z)
                for t in range(NT):
                    ins = pe.transpose(ps[0:NE, 5, P * t:P * (t + 1)], rt[:, 4, t], ident)
                ins.then_inc(ohT_ps, 1)
                pe.wait_ge(xT_ready, 5)
                for e in range(NE + 1):
                    if e < NE:
                        for f in range(4):
                            if e >= 1:
                                pe.wait_ge(relu_dve if f % 2 else relu_act, 2 * (e - 1) + f // 2 + 1)
                            pe.matmul(ps[:, f, :], w1_sb[:, e, P * f:P * (f + 1)], xnT, start=True, stop=True).then_inc(up_ready, 1)
                    if e >= 1:
                        d = e - 1
                        pe.wait_ge(relu_act, 2 * e)
                        pe.wait_ge(relu_dve, 2 * e)
                        if d == 1:
                            pe.wait_ge(ohT_ready, 1)
                        if d >= 2:
                            pe.wait_ge(comb_done, NT * (d - 1))
                        for t in range(NT):
                            for f in range(4):
                                ins = pe.matmul(ps[:, 4 + d % 2, P * t:P * (t + 1)], hE[:, d % 2, f, P * t:P * (t + 1)],
                                                w2_sb[:, d, f, :], start=(f == 0), stop=(f == 3))
                        ins.then_inc(down_ready, 1)
                pe.wait_ge(ohT_ready, 1)
                for t in range(NT):
                    ins = pe.matmul(ps[:, 6, P * t:P * (t + 1)], ohT[:, P * t:P * (t + 1)], b2_sb[:, :], start=True, stop=True)
                ins.then_inc(bias2_ready, 1)
                pe.wait_ge(bias2_ready, 1)
                pe.sem_inc(row_ended, 1)
                pe.wait_ge(row_opened[3], 1)
                pe.sem_clear(row_opened[3])


_INS = ["L0_attn_x", "L0_attn_w_qkv", "L0_attn_wo", "L0_attn_lambda_q1", "L0_attn_lambda_q2", "L0_attn_lambda_k1",
        "L0_attn_lambda_k2", "L0_attn_norm_w", "L0_ffn_w_gate", "L0_ffn_w_up", "L0_ffn_w_down", "L1_attn_Wq",
        "L1_attn_bq", "L1_attn_Wk", "L1_attn_bk", "L1_attn_Wv", "L1_attn_bv", "L1_attn_Wo", "L1_attn_bo", "L1_ffn_Wr",
        "L1_ffn_br", "L1_ffn_ln_g", "L1_ffn_ln_b", "L1_ffn_W1", "L1_ffn_b1", "L1_ffn_W2", "L1_ffn_b2"]


def shape_constants(np):
    p = np.arange(P)
    const = np.zeros((P, 3 * P + HF + 1 + NE), np.float32)
    const[:, 0:P] = np.eye(P)
    const[:, P:2 * P] = np.where(p[None, :] > p[:, None], NEG, 0)
    const[:, 2 * P:3 * P] = np.where(p[None, :] < p[:, None], NEG, 0)
    half = np.where(p < M_ROW, p % 16 // 4, (p - M_ROW) % 4)
    const[:, 3 * P:3 * P + HF] = (half[:, None] == np.arange(HF)) & (p < M_ROW + 12)[:, None]
    const[:, 3 * P + HF] = np.where(p % D1 < D1 // 2, -1, 1)
    const[:, 3 * P + HF + 1:] = NE - np.arange(NE)
    freq = np.float32(1.0) / np.float32(10000.0) ** (np.arange(0, D1, 2, dtype=np.float32) / np.float32(D1))
    angle = np.arange(T, dtype=np.float32)[None, :] * freq[p % (D1 // 2)][:, None]
    return const, np.stack([np.cos(angle), np.sin(angle)], 1).astype(np.float32)


def kernel(**inputs):
    import numpy as _np
    import concourse.bacc as _bacc
    from concourse import mybir as _mybir
    from concourse.bass_utils import run_bass_kernel_spmd as _run

    nc = _bacc.Bacc("TRN2", target_bir_lowering=False, num_devices=1)
    arrays, args = {}, []
    const, rope = shape_constants(_np)
    given = [(name, _np.ascontiguousarray(inputs[name])) for name in _INS] + [("const", const), ("rope", rope)]
    for name, a in given:
        arrays[f"in_{name}_dram"] = a
        args.append(nc.dram_tensor(f"in_{name}_dram", a.shape, _mybir.dt.from_np(a.dtype), kind="ExternalInput").ap())
    args.append(nc.dram_tensor("out_0_dram", (BATCH, T, E), F32, kind="ExternalOutput").ap())
    build(nc, *args)
    r = _run(nc, [arrays], core_ids=[0])
    return r.results[0]["out_0_dram"]
```
